# Optimizing a Trainium2 kernel written in Bass

```python
import numpy as np
import jax
import jax.numpy as jnp

def _softmax(x, axis=-1):
    return jax.nn.softmax(x, axis=axis)

def _gelu(x):
    return jax.nn.gelu(x, approximate=True)

def _silu(x):
    return jax.nn.silu(x)

def _sigmoid(x):
    return jax.nn.sigmoid(x)

def _layernorm(x, axis=-1, eps=1e-05):
    m = jnp.mean(x, axis=axis, keepdims=True)
    v = jnp.var(x, axis=axis, keepdims=True)
    return (x - m) / jnp.sqrt(v + eps)

def _scatter_add(tgt, idx, src, axis=0):
    return tgt.at[idx].add(src)

def _segment_sum(src, seg, n):
    return jax.ops.segment_sum(src, seg, n)
kernel_name = 'mk_gnn_preln_d1_gnn_r8_15a96f'

def setup_inputs(seed: int=0):
    np.random.seed(seed)
    _w = jnp.asarray

    def _rec_inputs():
        import jax
        import jax.numpy as jnp
        _gk = jax.random.key(seed)
        x = -0.0005121 + 1.001 * jax.random.normal(jax.random.fold_in(_gk, 1), (12500, 64), jnp.float32)
        _s = jax.random.randint(jax.random.fold_in(_gk, 2), (200000,), 0, 12500, jnp.int32)
        _d = jax.random.randint(jax.random.fold_in(_gk, 3), (200000,), 0, 12500, jnp.int32)
        _loop = jnp.arange(12500, dtype=jnp.int32)
        src = jnp.concatenate([_s, _d, _loop])
        dst = jnp.concatenate([_d, _s, _loop])
        _o = jnp.argsort(dst, stable=True)
        src = src[_o]
        dst = dst[_o]
        edge_attr_32 = -5.3897e-05 + 0.999841 * jax.random.normal(jax.random.fold_in(_gk, 11), (412500, 32), jnp.float32)
        return (x, src, dst, edge_attr_32)
    x, src, dst, edge_attr_32 = _rec_inputs()

    def _L0_gnn_setup():
        import jax, jax.numpy as jnp
        import numpy as np
        N = 6250
        E = 100000
        IN_DIM = 64
        OUT_DIM = 64
        PE_DIM = 32
        HID = 64
        gelu = lambda t: jax.nn.gelu(t, approximate=False)
        key = jax.random.key(seed)
        ks = jax.random.split(key, 12)

        def lin(k, fan_in, fan_out):
            bound = 1.0 / np.sqrt(fan_in)
            kw, kb = jax.random.split(k)
            W = jax.random.uniform(kw, (fan_in, fan_out), jnp.float32, -bound, bound)
            b = jax.random.uniform(kb, (fan_out,), jnp.float32, -bound, bound)
            return (W, b)
        x = jax.random.normal(ks[0], (N, IN_DIM), jnp.float32)
        pe_val = jax.random.normal(ks[1], (E, PE_DIM), jnp.float32)
        pe_index = jax.random.randint(ks[2], (2, E), 0, N, jnp.int64 if jax.config.jax_enable_x64 else jnp.int32)
        W0, b0 = lin(ks[3], PE_DIM, HID)
        W1, b1 = lin(ks[4], HID, HID)
        W2, b2 = lin(ks[5], HID, HID)
        W3, b3 = lin(ks[6], HID, IN_DIM)
        Wo, bo = lin(ks[7], IN_DIM, OUT_DIM)
        return {'x': x, 'pe_val': pe_val, 'pe_index': pe_index, 'W0': W0, 'b0': b0, 'W1': W1, 'b1': b1, 'W2': W2, 'b2': b2, 'W3': W3, 'b3': b3, 'Wo': Wo, 'bo': bo}
    _L0_gnn_all = _L0_gnn_setup()
    _L0_gnn_in = {k: v for k, v in _L0_gnn_all.items() if k in ('W0', 'b0', 'W1', 'b1', 'W2', 'b2', 'W3', 'b3', 'Wo', 'bo')}
    del _L0_gnn_all
    return {'x': x, 'src': src, 'dst': dst, 'edge_attr_32': edge_attr_32, 'L0_gnn_W0': _L0_gnn_in['W0'], 'L0_gnn_b0': _L0_gnn_in['b0'], 'L0_gnn_W1': _L0_gnn_in['W1'], 'L0_gnn_b1': _L0_gnn_in['b1'], 'L0_gnn_W2': _L0_gnn_in['W2'], 'L0_gnn_b2': _L0_gnn_in['b2'], 'L0_gnn_W3': _L0_gnn_in['W3'], 'L0_gnn_b3': _L0_gnn_in['b3'], 'L0_gnn_Wo': _L0_gnn_in['Wo'], 'L0_gnn_bo': _L0_gnn_in['bo']}

def reference(x, src, dst, edge_attr_32, L0_gnn_W0, L0_gnn_b0, L0_gnn_W1, L0_gnn_b1, L0_gnn_W2, L0_gnn_b2, L0_gnn_W3, L0_gnn_b3, L0_gnn_Wo, L0_gnn_bo):
    import jax
    import jax.numpy as jnp

    def _L0_gnn_ref(x, pe_val, pe_index, W0, b0, W1, b1, W2, b2, W3, b3, Wo, bo):
        import jax, jax.numpy as jnp
        import numpy as np
        N = 6250
        E = 100000
        IN_DIM = 64
        OUT_DIM = 64
        PE_DIM = 32
        HID = 64
        gelu = lambda t: jax.nn.gelu(t, approximate=False)
        h0 = pe_val @ W0 + b0
        h = gelu(h0) @ W1 + b1
        h = gelu(h) @ W2 + b2
        h0 = h0 + h
        score = h0 @ W3 + b3
        src, dst = (pe_index[0], pe_index[1])
        msg = x[src] * score
        n = x.shape[0]
        sums = jax.ops.segment_sum(msg, dst, num_segments=n)
        cnt = jax.ops.segment_sum(jnp.ones((msg.shape[0], 1), msg.dtype), dst, num_segments=n)
        wV = sums / jnp.maximum(cnt, 1.0)
        return wV @ Wo + bo
    edge_index = jnp.stack([src, dst])
    h = jnp.maximum(_layernorm(x, axis=-1), 0.0)
    x = x + _L0_gnn_ref(h, edge_attr_32, edge_index, L0_gnn_W0, L0_gnn_b0, L0_gnn_W1, L0_gnn_b1, L0_gnn_W2, L0_gnn_b2, L0_gnn_W3, L0_gnn_b3, L0_gnn_Wo, L0_gnn_bo)
    return x

_drawn_inputs = setup_inputs


def setup_inputs(seed=0):
    import zlib

    import numpy as np

    out = dict(_drawn_inputs(seed))
    spreads = {}
    factors = {'L0_gnn_b0': 4.477,
     'L0_gnn_W1': 8.0,
     'L0_gnn_b1': 8.0,
     'L0_gnn_W2': 8.0,
     'L0_gnn_b2': 4.844,
     'L0_gnn_b3': 3.051}
    for name, (base, spread) in spreads.items():
        noise = np.random.default_rng([zlib.crc32(name.encode()), seed]).standard_normal(out[name].shape)
        drawn = base * np.exp(spread * noise) if base else spread * noise
        out[name] = jnp.asarray(drawn.astype(out[name].dtype))
    for name, factor in factors.items():
        out[name] = (out[name] * factor).astype(out[name].dtype)
    return out
```

```python
from contextlib import ExitStack

import concourse.bass as bass
from concourse import mybir

F32 = mybir.dt.float32
I32 = mybir.dt.int32
ALU = mybir.AluOpType
ACT = mybir.ActivationFunctionType
AX_X = mybir.AxisListType.X

P = 128
N = 12500
D = 64
DE = 32
E = 412500
TILES = 8
HALF = TILES // 2 * P
BLOCK = TILES * P
NB = -(-E // BLOCK)
LAST_TILES = TILES // 2 + -(-(E - (NB - 1) * BLOCK - HALF) // P) if E > (NB - 1) * BLOCK + HALF else TILES
WIN = 64
DC = D + 1
NP = 125
NC = N // NP
EPS = 1e-5

G_RING = 8
IN_RING = 4
RAW = 6
LN_ROWS = 25
CHUNKS = -(-NB // P)

C_W1 = 0
C_W0 = C_W1 + P
C_FOLD = C_W0 + P
C_W3 = C_FOLD + D + DE + 1
C_B0 = C_W3 + D
C_B1 = C_B0 + 1
C_WO = C_B1 + 1
C_E = C_WO + DC
C_B3 = C_E + D + DE + 1
C_BO = C_B3 + D
C_ALL = C_BO + D


def edge_gated_layer(nc, x, edges, src, dst, dst_rows, weights, out):
    with ExitStack() as ctx:
        def sb(name, shape, dt=F32):
            return ctx.enter_context(nc.sbuf_tensor(name, shape, dt))

        def psum(name):
            return ctx.enter_context(nc.psum_tensor(name, [P, 512], F32))

        def sem(name):
            return ctx.enter_context(nc.semaphore(name))

        h_dram = nc.dram_tensor("h_rows", [N, D], F32, kind="Internal").ap()
        bounds_dram = nc.dram_tensor("block_bounds", [2, CHUNKS * P], I32, kind="Internal").ap()

        wp = sb("wp", [P, C_ALL])
        w_last = sb("w_last", [D + DE + 1, D])
        w1 = wp[:, C_W1:C_W1 + P]
        w0 = wp[0:2 * DE, C_W0:C_W0 + P]
        b0 = wp[:, C_B0:C_B0 + 1]
        b1 = wp[:, C_B1:C_B1 + 1]
        wo = wp[0:DC, C_WO:C_WO + DC]
        bo = wp[0:NP, C_BO:C_BO + D]
        xs = sb("xs", [NP, NC, D])
        acc = sb("acc", [DC, N + WIN])
        ln_d = sb("ln_d", [P, 4, LN_ROWS, D])
        ln_sq = sb("ln_sq", [P, 2, LN_ROWS, D])
        ln_sum = sb("ln_sum", [P, 4, LN_ROWS])
        ln_var = sb("ln_var", [P, 4, LN_ROWS])
        ln_std = sb("ln_std", [P, 4, LN_ROWS])
        dst_i = sb("dst_i", [P, NB, TILES], I32)
        dst_rel = dst_i[:, :, :].bitcast(F32)
        rows_i = sb("rows_i", [P, 2, BLOCK], I32)
        bounds = sb("bounds", [P, 2, CHUNKS], I32)
        base_b = sb("base_b", [P, NB], I32)
        top = sb("top", [1, NB], I32)
        span = sb("span", [1, NB], I32)
        widest = sb("widest", [1, 1], I32)
        iota_i = sb("iota_i", [P, WIN], I32)
        iota = sb("iota", [P, WIN])
        idx = sb("idx", [P, G_RING, TILES], I32)
        pair = sb("pair", [2 * DE, IN_RING, HALF])
        act_in = sb("act_in", [D + DE + 1, IN_RING, 2, HALF])
        g1 = sb("g1", [P, 2, HALF])
        rows = sb("rows", [P, G_RING, TILES, D])
        hot = sb("hot", [P, 2, TILES, WIN])
        msg = sb("msg", [P, 2, TILES, DC])
        fill = sb("fill", [P, 2])
        shifted = sb("shifted", [P, TILES])

        ps_h0 = [psum("ps_h0a"), psum("ps_h0b")]
        ps_h1 = [psum("ps_h1a"), psum("ps_h1b")]
        ps_s = [psum("ps_sa"), psum("ps_sb")]
        ps_w = [psum("ps_wa"), psum("ps_wb")]

        x_in = [sem(f"x_in{c}") for c in range(4)]
        weights_in = sem("weights_in")
        rows_in = [sem(f"rows_in{c}") for c in range(2)]
        bounds_out = sem("bounds_out")
        base_in = sem("base_in")
        dst_in = sem("dst_in")
        h_out = sem("h_out")
        y_out = sem("y_out")
        set_up = sem("set_up")
        fill_ready = sem("fill_ready")
        ones_ready = sem("ones_ready")
        acc_zero = sem("acc_zero")
        ln_step = sem("ln_step")
        ln_centred = sem("ln_centred")
        ln_squared = sem("ln_squared")
        ln_var_ready = sem("ln_var_ready")
        ln_std_ready = sem("ln_std_ready")
        h_ready = sem("h_ready")
        raw_ready = sem("raw_ready")
        fold_done = sem("fold_done")
        w_last_ready = sem("w_last_ready")
        bounds_step = sem("bounds_step")
        bounds_ready = sem("bounds_ready")
        plan_ready = sem("plan_ready")
        pair_in = [sem(f"pair_in{s}") for s in range(IN_RING)]
        attr_in = [sem(f"attr_in{s}") for s in range(IN_RING)]
        idx_in = [sem(f"idx_in{s}") for s in range(G_RING)]
        gathered = [sem(f"gathered{s}") for s in range(G_RING)]
        h0_done = sem("h0_done")
        g1_done = sem("g1_done")
        h1_done = sem("h1_done")
        g2_done = sem("g2_done")
        score_done = sem("score_done")
        gathers_begun = sem("gathers_begun")
        added = sem("added")
        msg_done = sem("msg_done")
        sums_done = sem("sums_done")
        acc_done = sem("acc_done")
        win_hot = sem("win_hot")
        win_shift = sem("win_shift")
        windows_ended = sem("windows_ended")
        win_sums = sem("win_sums")
        x_biased = sem("x_biased")
        proj_done = sem("proj_done")
        cnt_ready = sem("cnt_ready")
        y_mul = sem("y_mul")
        y_ready = sem("y_ready")

        x_nodes = x.rearrange("(p c) d -> p c d", p=NP)
        h_nodes = h_dram.rearrange("(p c) d -> p c d", p=NP)
        y_nodes = out.rearrange("(p c) d -> p c d", p=NP)
        LN_STEPS = NC // LN_ROWS
        jobs = [(LN_ROWS, NP)] * LN_STEPS + [(2 * TILES, P)] * (RAW // 2)
        ln_y = ln_d[0:NP, :, :, :].rearrange("p k n d -> p (k n) d")
        PER = 512 // DC
        groups = [(c, min(PER, NC - c)) for c in range(0, NC, PER)]
        banks = [ps_h0[0], ps_h1[0], ps_h0[1], ps_h1[1]]

        def blocks_loop(eng, first, end, unroll, step):
            turns = (end - first) // unroll
            with eng.Fori(0, turns) as i:
                for u in range(unroll):
                    step(i * unroll + (first + u), first + u)
            for b in range(first + turns * unroll, end):
                step(b, b)

        def uses(b, ring):
            return (b >> ring.bit_length() - 1) + 1

        def tiles_of(b):
            return LAST_TILES if isinstance(b, int) and b == NB - 1 else TILES

        block = ctx.enter_context(nc.Block())

        @block.sync
        def _(sp):
            def load_idx(b, s):
                sp.dma_start(idx[:, s % G_RING, :], src[one(b), :, :].rearrange("o p t -> p (o t)")
                             ).then_inc(idx_in[s % G_RING], 16)

            def load_pair(b, s):
                sp.dma_start(pair[:, s % IN_RING, :],
                             edges[one(b), :, :, :].rearrange("o g f j -> (o g f) j")
                             ).then_inc(pair_in[s % IN_RING], 16)

            def load_attr(b, s):
                sp.dma_start(act_in[D:D + DE, s % IN_RING, :, :],
                             edges[one(b), :, :, :].rearrange("o g f j -> f (o g) j")
                             ).then_inc(attr_in[s % IN_RING], 16)

            load_idx(0, 0)
            for c in range(LN_STEPS):
                cols = slice(c * LN_ROWS, (c + 1) * LN_ROWS)
                sp.dma_start(xs[:, cols, :], x_nodes[:, cols, :]).then_inc(x_in[c], 16)
            for b in range(1, G_RING):
                load_idx(b, b)
            sp.dma_start(wp[:, :], weights).then_inc(weights_in, 16)
            for b in range(2):
                load_pair(b, b)
                load_attr(b, b)
            sp.dma_start(dst_i[:, :, :], dst).then_inc(dst_in, 16)
            for c in range(CHUNKS):
                n = len(range(c, NB, CHUNKS))
                if c >= 2:
                    sp.wait_ge(bounds_step, 1 + 2 * (c - 1))
                sp.dma_start(rows_i[0:n, c % 2, :], dst_rows[c:NB:CHUNKS, :]
                             ).then_inc(rows_in[c % 2], 16)
            for b in range(2, IN_RING):
                load_pair(b, b)
                load_attr(b, b)
            sp.wait_ge(bounds_step, 1 + 2 * CHUNKS)
            sp.dma_start(bounds_dram.rearrange("m (p c) -> p m c", p=P), bounds[:, :, :]
                         ).then_inc(bounds_out, 16)
            sp.wait_ge(bounds_out, 16)
            sp.dma_start(base_b[:, :], bounds_dram[0:1, 0:NB].broadcast_to([P, NB])
                         ).then_inc(base_in, 16)
            sp.dma_start(top[:, :], bounds_dram[1:2, 0:NB]).then_inc(base_in, 16)

            def ahead(b, s):
                sp.wait_ge(h0_done, b + 1)
                load_pair(b + IN_RING, s + IN_RING)
                sp.wait_ge(score_done, b + 1)
                load_attr(b + IN_RING, s + IN_RING)

            def ahead_all(b, s):
                ahead(b, s)
                sp.wait_ge(gathered[s % G_RING], uses(b, G_RING) * 16 * TILES)
                load_idx(b + G_RING, s + G_RING)

            blocks_loop(sp, 0, NB - G_RING, G_RING, ahead_all)
            for b in range(NB - G_RING, NB - IN_RING):
                ahead(b, b)

            done = 0
            for q in range(4):
                upto = (len(groups) * (q + 1)) // 4
                sp.wait_ge(y_ready, upto)
                c0 = groups[done][0]
                c1 = groups[upto - 1][0] + groups[upto - 1][1]
                sp.dma_start(y_nodes[:, c0:c1, :], ln_y[:, c0:c1, :]).then_inc(y_out, 16)
                done = upto
            sp.wait_ge(y_out, 16 * 4)
            sp.wait_ge(h_out, 16 * LN_STEPS)

        @block.gpsimd
        def _(pool):
            pool.iota(iota_i[:, :], pattern=[[1, WIN]], base=0, channel_multiplier=0
                      ).then_inc(set_up, 1)

            def gather(b, s, table):
                slot = s % G_RING
                pool.wait_ge(idx_in[slot], uses(b, G_RING) * 16)
                pool.sem_inc(gathers_begun, 1)
                for t in range(tiles_of(b)):
                    pool.indirect_dma_start(
                        rows[:, slot, t, :], None, table,
                        bass.IndirectOffsetOnAxis(ap=idx[:, slot, t:t + 1], axis=0),
                    ).then_inc(gathered[slot], 16)

            for b in range(RAW):
                gather(b, b, x)
            pool.wait_ge(h_out, 16 * LN_STEPS)
            for b in range(RAW, G_RING):
                gather(b, b, h_dram)

            def gather_ahead(b, s):
                pool.wait_ge(msg_done, b + 1)
                gather(b + G_RING, s + G_RING, h_dram)

            blocks_loop(pool, 0, NB - G_RING, G_RING, gather_ahead)

            for k, (c, n) in enumerate(groups):
                pool.wait_ge(y_mul, k + 1)
                if k == 0:
                    pool.wait_ge(x_biased, 1)
                pool.tensor_tensor(ln_y[:, c:c + n, :], ln_y[:, c:c + n, :], xs[:, c:c + n, :],
                                   ALU.add).then_inc(y_ready, 1)

        @block.scalar
        def _(act):
            def ln_act(k, n, parts):
                act.wait_ge(ln_centred, k + 1)
                if k >= 2:
                    act.wait_ge(ln_var_ready, k - 1)
                act.activation(ln_sq[0:parts, k % 2, 0:n, :], ln_d[0:parts, k % 4, 0:n, :],
                               ACT.Square).then_inc(ln_squared, 1)

            def ln_root(k, n, parts):
                act.wait_ge(ln_var_ready, k + 1)
                act.activation(ln_std[0:parts, k % 4, 0:n], ln_var[0:parts, k % 4, 0:n],
                               ACT.Sqrt).then_inc(ln_std_ready, 1)

            def store_h(k):
                act.wait_ge(h_ready, k + 1)
                cols = slice(k * LN_ROWS, (k + 1) * LN_ROWS)
                act.dma_start(h_nodes[:, cols, :], ln_d[0:NP, k % 4, :, :]).then_inc(h_out, 16)

            act.wait_ge(fill_ready, 1)
            act.activation(act_in[D + DE:D + DE + 1, :, :, :].rearrange("p s g j -> p (s g j)"),
                           fill[D + DE:D + DE + 1, 1:2].to_broadcast([1, IN_RING * 2 * HALF]),
                           ACT.Copy).then_inc(ones_ready, 1)
            for k in range(LN_STEPS + 1):
                if k < LN_STEPS:
                    ln_act(k, *jobs[k])
                if k >= 1:
                    ln_root(k - 1, *jobs[k - 1])
                if k >= 2:
                    store_h(k - 2)
            store_h(LN_STEPS - 1)
            act.activation(acc[:, :], fill[0:DC, 0:1].to_broadcast([DC, N + WIN]), ACT.Copy
                           ).then_inc(acc_zero, 1)
            for k in range(LN_STEPS, len(jobs)):
                ln_act(k, *jobs[k])
                ln_root(k, *jobs[k])
            act.wait_ge(weights_in, 16)

            def gelus(b, s):
                act.wait_ge(h0_done, b + 1)
                act.activation(g1[:, s % 2, :], ps_h0[s % 2][:, :], ACT.Gelu, bias=b0
                               ).then_inc(g1_done, 1)
                act.wait_ge(h1_done, b + 1)
                for g in range(2):
                    act.activation(act_in[0:D, s % IN_RING, g, :],
                                   ps_h1[s % 2][g * D:(g + 1) * D, :], ACT.Gelu,
                                   bias=wp[g * D:(g + 1) * D, C_B1:C_B1 + 1]
                                   ).then_inc(g2_done, 1)

            blocks_loop(act, 0, NB, IN_RING, gelus)

        @block.tensor
        def _(pe):
            pe.wait_ge(weights_in, 16)
            pe.matmul(ps_s[0][0:D + DE + 1, 0:D], wp[:, C_FOLD:C_FOLD + D + DE + 1],
                      wp[:, C_W3:C_W3 + D], start=True, stop=False)
            pe.matmul(ps_s[0][0:D + DE + 1, 0:D], wp[0:1, C_E:C_E + D + DE + 1],
                      wp[0:1, C_B3:C_B3 + D], start=False, stop=True).then_inc(fold_done, 1)
            pe.wait_ge(w_last_ready, 1)
            pe.wait_ge(ones_ready, 1)

            def first(b, s):
                pe.wait_ge(pair_in[s % IN_RING], uses(b, IN_RING) * 16)
                pe.matmul(ps_h0[s % 2][:, :], w0, pair[:, s % IN_RING, :], start=True, stop=True
                          ).then_inc(h0_done, 1)

            def second(b, s):
                pe.wait_ge(g1_done, b + 1)
                pe.matmul(ps_h1[s % 2][:, :], w1, g1[:, s % 2, :], start=True, stop=True
                          ).then_inc(h1_done, 1)

            def last(b, s):
                pe.wait_ge(attr_in[s % IN_RING], uses(b, IN_RING) * 16)
                pe.wait_ge(g2_done, (b + 1) * 2)
                for t in range(TILES):
                    g, j = t % 2, t // 2
                    mm = pe.matmul(ps_s[s % 2][:, t * D:(t + 1) * D],
                                   act_in[:, s % IN_RING, g, j * P:(j + 1) * P],
                                   w_last[:, :], start=(t == 0), stop=(t == TILES - 1),
                                   skip_group_check=True)
                mm.then_inc(score_done, 1)

            def sums(b, s, window, onehot):
                n = tiles_of(b)
                for t in range(n):
                    last = pe.matmul(window, msg[:, s % 2, t, :], onehot[:, t, :],
                                     start=(t == 0), stop=(t == n - 1))
                return last

            def narrow(b, s):
                pe.wait_ge(msg_done, b + 1)
                sums(b, s, ps_w[s % 2][0:DC, 0:WIN], hot[:, s % 2, :, :]).then_inc(sums_done, 1)

            def wide(b, s):
                pe.wait_ge(msg_done, b + 1)
                spanned = pe.value_load(span[0:1, one(b)], min_val=0, max_val=N)
                with pe.Fori(0, (spanned >> 6) + 1) as w:
                    pe.wait_ge(win_hot, w + 1)
                    sums(b, s, ps_w[0][0:DC, 0:WIN], hot[:, 0, :, :]).then_inc(win_sums, 1)

            def program(summed):
                first(0, 0)
                second(0, 0)
                first(1, 1)
                last(0, 0)

                def step(b, s):
                    second(b, s)
                    first(b + 1, s + 1)
                    summed(b - 1, s - 1)
                    last(b, s)

                blocks_loop(pe, 1, NB - 1, IN_RING, step)
                second(NB - 1, NB - 1)
                summed(NB - 2, NB - 2)
                last(NB - 1, NB - 1)
                summed(NB - 1, NB - 1)

            pe.wait_ge(plan_ready, 1)
            flag = pe.value_load(widest[0:1, 0:1], min_val=0, max_val=N)
            with pe.If(flag < WIN):
                program(narrow)
            with pe.Else():
                program(wide)

            pe.wait_ge(acc_done, 1)
            for k, (c, n) in enumerate(groups):
                if k >= len(banks):
                    pe.wait_ge(y_mul, k - len(banks) + 1)
                for j in range(n):
                    last = pe.matmul(banks[k % 4][0:NP, j * DC:(j + 1) * DC],
                                     acc[:, c + j:c + j + (NP - 1) * NC + 1:NC], wo,
                                     start=(j == 0), stop=(j == n - 1), skip_group_check=True)
                last.then_inc(proj_done, 1)

        @block.vector
        def _(dve):
            own = [0]

            def chained(ins):
                own[0] += 1
                ins.then_inc(ln_step, 1)
                dve.wait_ge(ln_step, own[0])

            dve.memset(fill[:, 0:1], 0.0)
            dve.memset(fill[:, 1:2], 1.0).then_inc(fill_ready, 1)
            dve.memset(msg[:, :, :, D:DC], 1.0)
            dve.memset(bounds[:, :, :], 0).then_inc(bounds_step, 1)
            dve.wait_ge(set_up, 1)
            dve.tensor_copy(iota[:, :], iota_i[:, :]).then_inc(set_up, 1)

            def source(k):
                if k < LN_STEPS:
                    return xs[:, k * LN_ROWS:(k + 1) * LN_ROWS, :]
                n = jobs[k][0]
                flat = rows[:, 0:RAW, :, :].rearrange("p b t d -> p (b t) d")
                return flat[:, (k - LN_STEPS) * n:(k - LN_STEPS + 1) * n, :]

            def centre(k):
                n, parts = jobs[k]
                d, s = ln_d[0:parts, k % 4, 0:n, :], ln_sum[0:parts, k % 4, 0:n]
                if k < LN_STEPS:
                    dve.wait_ge(x_in[k], 16)
                else:
                    per = RAW // (len(jobs) - LN_STEPS)
                    for b in range((k - LN_STEPS) * per, (k - LN_STEPS + 1) * per):
                        dve.wait_ge(gathered[b], 16 * TILES)
                    dve.wait_ge(h_out, 16 * LN_STEPS)
                chained(dve.tensor_reduce(s, source(k), AX_X, ALU.add))
                chained(dve.tensor_scalar(s, s, 1.0 / D, None, ALU.mult))
                dve.tensor_tensor(d, source(k), s.unsqueeze(2).to_broadcast([parts, n, D]),
                                  ALU.subtract).then_inc(ln_centred, 1)

            def variance(k):
                n, parts = jobs[k]
                v = ln_var[0:parts, k % 4, 0:n]
                dve.wait_ge(ln_squared, k + 1)
                chained(dve.tensor_reduce(v, ln_sq[0:parts, k % 2, 0:n, :], AX_X, ALU.add))
                dve.tensor_scalar(v, v, 1.0 / D, EPS, ALU.mult, ALU.add).then_inc(ln_var_ready, 1)

            def finish(k):
                n, parts = jobs[k]
                d, r = ln_d[0:parts, k % 4, 0:n, :], ln_std[0:parts, k % 4, 0:n]
                dve.wait_ge(ln_std_ready, k + 1)
                dve.wait_ge(ln_centred, k + 1)
                chained(dve.reciprocal(r, r))
                to = d if k < LN_STEPS else source(k)
                dve.scalar_tensor_tensor(out=to, in0=d, scalar=0.0,
                                         in1=r.unsqueeze(2).to_broadcast([parts, n, D]),
                                         op0=ALU.max, op1=ALU.mult
                                         ).then_inc(h_ready if k < LN_STEPS else raw_ready, 1)

            centre(0)
            for k in range(LN_STEPS):
                if k + 1 < LN_STEPS:
                    centre(k + 1)
                variance(k)
                finish(k)

            for c in range(CHUNKS):
                n = len(range(c, NB, CHUNKS))
                dve.wait_ge(rows_in[c % 2], 16 * (c // 2 + 1))
                if c == 0:
                    dve.wait_ge(bounds_step, 1)
                dve.tensor_reduce(bounds[0:n, 0, c:c + 1], rows_i[0:n, c % 2, :], AX_X, ALU.min
                                  ).then_inc(bounds_step, 1)
                dve.tensor_reduce(bounds[0:n, 1, c:c + 1], rows_i[0:n, c % 2, :], AX_X, ALU.max
                                  ).then_inc(bounds_step, 1)
            dve.wait_ge(fold_done, 1)
            dve.tensor_copy(w_last[:, :], ps_s[0][0:D + DE + 1, 0:D]).then_inc(w_last_ready, 1)

            for k in range(LN_STEPS, len(jobs)):
                centre(k)
                variance(k)
                finish(k)

            dve.wait_ge(base_in, 32)
            chained(dve.tensor_tensor(span[:, :], top[:, :], base_b[0:1, :], ALU.subtract))
            dve.tensor_reduce(widest[:, :], span[:, :], AX_X, ALU.max).then_inc(plan_ready, 1)
            dve.wait_ge(dst_in, 16)
            chained(dve.tensor_tensor(dst_rel, dst_i[:, :, :],
                                      base_b[:, :].unsqueeze(2).to_broadcast([P, NB, TILES]),
                                      ALU.subtract))
            dve.wait_ge(acc_zero, 1)
            dve.wait_ge(set_up, 2)
            dve.wait_ge(raw_ready, len(jobs) - LN_STEPS)
            dve.wait_ge(plan_ready, 1)

            def bias_residual():
                dve.tensor_tensor(xs[:, :, :], xs[:, :, :],
                                  bo.unsqueeze(1).to_broadcast([NP, NC, D]), ALU.add
                                  ).then_inc(x_biased, 1)

            iota_tiles = iota[:, :].unsqueeze(1).to_broadcast([P, TILES, WIN])

            def one_hot(to, rel):
                return dve.tensor_tensor(to, rel.unsqueeze(2).to_broadcast([P, TILES, WIN]),
                                         iota_tiles, ALU.is_equal)

            def message(b, s):
                dve.wait_ge(score_done, b + 1)
                n = tiles_of(b)
                dve.wait_ge(gathered[s % G_RING], (uses(b, G_RING) - 1) * 16 * TILES + 16 * n)
                dve.tensor_tensor(msg[:, s % 2, 0:n, 0:D],
                                  ps_s[s % 2][:, 0:n * D].rearrange("p (t d) -> p t d", d=D),
                                  rows[:, s % G_RING, 0:n, :], ALU.mult).then_inc(msg_done, 1)

            def rel_of(b):
                return dst_rel[:, one(b), :].rearrange("p o t -> p (o t)")

            def add_window(b, s):
                base = dve.value_load(base_b[0:1, one(b)], min_val=0, max_val=N - 1)
                dve.wait_ge(sums_done, b + 1)
                if s > 0:
                    dve.wait_ge(added, b)
                place = acc[:, bass.ds(base, WIN)]
                dve.tensor_tensor(place, place, ps_w[s % 2][0:DC, 0:WIN], ALU.add
                                  ).then_inc(added, 1)

            def narrow(b, s):
                one_hot(hot[:, s % 2, :, :], rel_of(b))
                message(b, s)

            def program_narrow():
                narrow(0, 0)
                narrow(1, 1)
                add_window(0, 0)
                bias_residual()

                def step(b, s):
                    narrow(b, s)
                    add_window(b - 1, s - 1)

                blocks_loop(dve, 2, NB, G_RING, step)
                add_window(NB - 1, NB - 1)
                dve.wait_ge(added, NB)

            def wide(b, s):
                message(b, s)
                base = dve.value_load(base_b[0:1, one(b)], min_val=0, max_val=N - 1)
                spanned = dve.value_load(span[0:1, one(b)], min_val=0, max_val=N)
                dve.tensor_copy(shifted[:, :], rel_of(b)).then_inc(win_shift, 1)
                with dve.Fori(0, (spanned >> 6) + 1) as w:
                    dve.wait_ge(win_shift, w * 2 + 1)
                    one_hot(hot[:, 0, :, :], shifted[:, :]).then_inc(win_hot, 1)
                    dve.wait_ge(win_hot, w + 1)
                    dve.tensor_scalar(shifted[:, :], shifted[:, :], float(-WIN), None, ALU.add
                                      ).then_inc(win_shift, 1)
                    dve.wait_ge(win_sums, w + 1)
                    at = nc.s_assert_within(
                        base + w * WIN, min_val=0, max_val=N,
                        skip_runtime_bounds_check_because="w * WIN is at most the block's span")
                    place = acc[:, bass.ds(at, WIN)]
                    dve.tensor_tensor(place, place, ps_w[0][0:DC, 0:WIN], ALU.add
                                      ).then_inc(win_shift, 1)
                dve.wait_ge(win_shift, ((spanned >> 6) + 1) * 2 + 1)
                dve.sem_inc(windows_ended, 1)
                dve.sem_clear(win_shift)
                dve.sem_clear(win_hot)
                dve.sem_clear(win_sums)

            flag = dve.value_load(widest[0:1, 0:1], min_val=0, max_val=N)
            with dve.If(flag < WIN):
                program_narrow()
            with dve.Else():
                bias_residual()
                blocks_loop(dve, 0, NB, G_RING, wide)

            dve.sem_inc(acc_done, 1)
            for k, (c, n) in enumerate(groups):
                dve.wait_ge(proj_done, k + 1)
                got = banks[k % 4][0:NP, 0:n * DC].rearrange("p (j d) -> p j d", d=DC)
                cnt = ln_sum[0:NP, k % 4, 0:n]
                chained(dve.tensor_scalar(cnt.unsqueeze(2), got[:, :, D:DC], 1.0, None, ALU.max))
                chained(dve.reciprocal(cnt, cnt))
                dve.tensor_tensor(ln_y[:, c:c + n, :], got[:, :, 0:D],
                                  cnt.unsqueeze(2).to_broadcast([NP, n, D]), ALU.mult
                                  ).then_inc(y_mul, 1)


def one(b):
    return bass.ds(b, 1)


def kernel(x, src, dst, edge_attr_32, L0_gnn_W0, L0_gnn_b0, L0_gnn_W1, L0_gnn_b1, L0_gnn_W2,
           L0_gnn_b2, L0_gnn_W3, L0_gnn_b3, L0_gnn_Wo, L0_gnn_bo):
    import numpy as np
    import concourse.bacc as bacc
    from concourse.bass_utils import run_bass_kernel_spmd

    def padded(a, value):
        out = np.full((NB * BLOCK, *a.shape[1:]), value, a.dtype)
        out[:E] = a
        return out

    src, dst = np.asarray(src), np.asarray(dst)
    edges = padded(np.asarray(edge_attr_32), 0).reshape(NB, 2, HALF, DE).transpose(0, 1, 3, 2)
    tiled = lambda a: a.reshape(NB, 2, TILES // 2, P).transpose(0, 3, 2, 1).reshape(NB, P, TILES)
    dst_all = padded(dst, N)

    w = np.zeros((P, C_ALL), np.float32)
    for g in range(2):
        w[g * D:(g + 1) * D, C_W1 + g * D:C_W1 + (g + 1) * D] = L0_gnn_W1
        w[g * DE:(g + 1) * DE, C_W0 + g * D:C_W0 + (g + 1) * D] = L0_gnn_W0
        w[g * D:(g + 1) * D, C_W3:C_W3 + D] = L0_gnn_W3
        w[g * D:(g + 1) * D, C_B0] = L0_gnn_b0
        w[g * D:(g + 1) * D, C_B1] = L0_gnn_b1
    w[0:D, C_FOLD:C_FOLD + D] = np.asarray(L0_gnn_W2).T
    w[0:D, C_FOLD + D:C_FOLD + D + DE] = np.asarray(L0_gnn_W0).T
    w[0:D, C_FOLD + D + DE] = L0_gnn_b0
    w[D:2 * D, C_FOLD + D + DE] = L0_gnn_b2
    w[0:D, C_WO:C_WO + D] = L0_gnn_Wo
    w[D, C_WO + D] = 1.0
    w[0, C_E + D + DE] = 1.0
    w[0, C_B3:C_B3 + D] = L0_gnn_b3
    w[:, C_BO:C_BO + D] = L0_gnn_bo

    arrays = {
        "x": np.ascontiguousarray(x),
        "edges": np.ascontiguousarray(edges),
        "src": np.ascontiguousarray(tiled(padded(src, 0))),
        "dst": np.ascontiguousarray(tiled(dst_all).transpose(1, 0, 2)),
        "dst_rows": dst_all.reshape(NB, BLOCK),
        "weights": w,
    }
    nc = bacc.Bacc("TRN2", target_bir_lowering=False, num_devices=1)
    args = {n: nc.dram_tensor(f"in_{n}", a.shape, mybir.dt.from_np(a.dtype), kind="ExternalInput").ap()
            for n, a in arrays.items()}
    out = nc.dram_tensor("out", (N, D), F32, kind="ExternalOutput").ap()
    edge_gated_layer(nc, **args, out=out)
    got = run_bass_kernel_spmd(nc, [{f"in_{n}": a for n, a in arrays.items()}], core_ids=[0])
    return got.results[0]["out"]
```

```python
from contextlib import ExitStack

import concourse.bass as bass
from concourse import mybir

F32 = mybir.dt.float32
I32 = mybir.dt.int32
ALU = mybir.AluOpType
ACT = mybir.ActivationFunctionType
AX_X = mybir.AxisListType.X

P = 128
N = 12500
D = 64
DE = 32
E = 412500
TILES = 8
HALF = TILES // 2 * P
BLOCK = TILES * P
NB = -(-E // BLOCK)
LAST_TILES = TILES - (NB * BLOCK - E) // P
assert LAST_TILES >= TILES - 1
WIN = 64
DC = D + 1
NP = 125
NC = N // NP
LATE_TILES = 4
N_EARLY = N - LATE_TILES * NP
EP = N_EARLY // NC
EARLY_BLOCKS = -(-NB * (N_EARLY + NP) // N)
EPS = 1e-5

G_RING = 8
IN_RING = 4
RAW = 6
LN_ROWS = 25
CHUNKS = -(-NB // P)

C_W1 = 0
C_W0 = C_W1 + P
C_FOLD = C_W0 + P
C_W3 = C_FOLD + D + DE + 1
C_B0 = C_W3 + D
C_B1 = C_B0 + 1
C_WO = C_B1 + 1
C_E = C_WO + DC
C_B3 = C_E + D + DE + 1
C_BO = C_B3 + D
C_ALL = C_BO + D


def edge_gated_layer(nc, x, edges, src, dst, dst_rows, weights, out):
    with ExitStack() as ctx:
        def sb(name, shape, dt=F32):
            return ctx.enter_context(nc.sbuf_tensor(name, shape, dt))

        def psum(name):
            return ctx.enter_context(nc.psum_tensor(name, [P, 512], F32))

        def sem(name):
            return ctx.enter_context(nc.semaphore(name))

        h_dram = nc.dram_tensor("h_rows", [N, D], F32, kind="Internal").ap()
        bounds_dram = nc.dram_tensor("block_bounds", [2, CHUNKS * P], I32, kind="Internal").ap()

        wp = sb("wp", [P, C_ALL])
        w_last = sb("w_last", [D + DE + 1, D])
        w1 = wp[:, C_W1:C_W1 + P]
        w0 = wp[0:2 * DE, C_W0:C_W0 + P]
        b0 = wp[:, C_B0:C_B0 + 1]
        wo = wp[0:DC, C_WO:C_WO + DC]
        bo = wp[0:NP, C_BO:C_BO + D]
        xs = sb("xs", [NP, NC, D])
        x_late = sb("x_late", [NP, LATE_TILES, D])
        y_late = sb("y_late", [NP, LATE_TILES, D])
        acc = sb("acc", [DC, N + WIN])
        ln_d = sb("ln_d", [P, 4, LN_ROWS, D])
        ln_sq = sb("ln_sq", [P, 2, LN_ROWS, D])
        ln_sum = sb("ln_sum", [P, 4, LN_ROWS])
        ln_var = sb("ln_var", [P, 4, LN_ROWS])
        ln_std = sb("ln_std", [P, 4, LN_ROWS])
        dst_i = sb("dst_i", [P, NB, TILES], I32)
        dst_rel = dst_i[:, :, :].bitcast(F32)
        rows_i = sb("rows_i", [P, 2, BLOCK], I32)
        bounds = sb("bounds", [P, 2, CHUNKS], I32)
        base_b = sb("base_b", [P, NB], I32)
        top = sb("top", [1, NB], I32)
        span = sb("span", [1, NB], I32)
        late = sb("late", [1, 1], I32)
        widest = sb("widest", [1, 1], I32)
        iota_i = sb("iota_i", [P, WIN], I32)
        iota = sb("iota", [P, WIN])
        idx = sb("idx", [P, G_RING, TILES], I32)
        pair = sb("pair", [2 * DE, IN_RING, HALF])
        act_in = sb("act_in", [D + DE + 1, IN_RING, 2, HALF])
        g1 = sb("g1", [P, 2, HALF])
        rows = sb("rows", [P, G_RING, TILES, D])
        hot = sb("hot", [P, 2, TILES, WIN])
        msg = sb("msg", [P, 2, TILES, DC])
        fill = sb("fill", [P, 2])
        shifted = sb("shifted", [P, TILES])

        ps_h0 = [psum("ps_h0a"), psum("ps_h0b")]
        ps_h1 = [psum("ps_h1a"), psum("ps_h1b")]
        ps_s = [psum("ps_sa"), psum("ps_sb")]
        ps_w = [psum("ps_wa"), psum("ps_wb")]

        x_in = [sem(f"x_in{c}") for c in range(4)]
        x_late_in = sem("x_late_in")
        weights_in = sem("weights_in")
        rows_in = [sem(f"rows_in{c}") for c in range(2)]
        bounds_out = sem("bounds_out")
        base_in = sem("base_in")
        dst_in = sem("dst_in")
        h_out = sem("h_out")
        y_out = sem("y_out")
        set_up = sem("set_up")
        fill_ready = sem("fill_ready")
        ones_ready = sem("ones_ready")
        acc_zero = sem("acc_zero")
        ln_step = sem("ln_step")
        ln_centred = sem("ln_centred")
        ln_squared = sem("ln_squared")
        ln_var_ready = sem("ln_var_ready")
        ln_std_ready = sem("ln_std_ready")
        h_ready = sem("h_ready")
        raw_ready = sem("raw_ready")
        fold_done = sem("fold_done")
        w_last_ready = sem("w_last_ready")
        bounds_step = sem("bounds_step")
        bounds_ready = sem("bounds_ready")
        plan_ready = sem("plan_ready")
        pair_in = [sem(f"pair_in{s}") for s in range(IN_RING)]
        attr_in = [sem(f"attr_in{s}") for s in range(IN_RING)]
        idx_in = [sem(f"idx_in{s}") for s in range(G_RING)]
        gathered = [sem(f"gathered{s}") for s in range(G_RING)]
        h0_done = sem("h0_done")
        g1_done = sem("g1_done")
        h1_done = sem("h1_done")
        g2_done = sem("g2_done")
        score_done = sem("score_done")
        gathers_begun = sem("gathers_begun")
        first_hot = sem("first_hot")
        added = sem("added")
        msg_done = sem("msg_done")
        sums_done = sem("sums_done")
        acc_done = sem("acc_done")
        win_hot = sem("win_hot")
        win_shift = sem("win_shift")
        windows_ended = sem("windows_ended")
        win_sums = sem("win_sums")
        x_biased = sem("x_biased")
        proj_done = sem("proj_done")
        cnt_ready = sem("cnt_ready")
        y_mul = sem("y_mul")
        y_ready = sem("y_ready")

        x_nodes = x.rearrange("(p c) d -> p c d", p=NP)
        h_nodes = h_dram.rearrange("(p c) d -> p c d", p=NP)
        y_nodes = out[0:N_EARLY, :].rearrange("(p c) d -> p c d", p=EP)
        LN_STEPS = NC // LN_ROWS
        jobs = [(LN_ROWS, NP)] * LN_STEPS + [(2 * TILES, P)] * (RAW // 2)
        ln_y = ln_d[0:EP, :, :, :].rearrange("p k n d -> p (k n) d")
        PER = 512 // DC
        groups = [(c, min(PER, NC - c)) for c in range(0, NC, PER)]

        def blocks_loop(eng, first, end, unroll, step):
            turns = (end - first) // unroll
            if turns < 2:
                turns = 0
            else:
                with eng.Fori(0, turns) as i:
                    for u in range(unroll):
                        step(i * unroll + (first + u), first + u)
            for b in range(first + turns * unroll, end):
                step(b, b)

        def uses(b, ring):
            return (b >> ring.bit_length() - 1) + 1

        def tiles_of(b):
            return LAST_TILES if isinstance(b, int) and b == NB - 1 else TILES

        block = ctx.enter_context(nc.Block())

        @block.sync
        def _(sp):
            def load_idx(b, s):
                sp.dma_start(idx[:, s % G_RING, :], src[one(b), :, :].rearrange("o p t -> p (o t)")
                             ).then_inc(idx_in[s % G_RING], 16)

            def load_pair(b, s):
                sp.dma_start(pair[:, s % IN_RING, :],
                             edges[one(b), :, :, :].rearrange("o g f j -> (o g f) j")
                             ).then_inc(pair_in[s % IN_RING], 16)

            def load_attr(b, s):
                sp.dma_start(act_in[D:D + DE, s % IN_RING, :, :],
                             edges[one(b), :, :, :].rearrange("o g f j -> f (o g) j")
                             ).then_inc(attr_in[s % IN_RING], 16)

            load_idx(0, 0)
            load_idx(1, 1)
            for c in range(LN_STEPS):
                cols = slice(c * LN_ROWS, (c + 1) * LN_ROWS)
                sp.dma_start(xs[:, cols, :], x_nodes[:, cols, :]).then_inc(x_in[c], 16)
            for b in range(2, G_RING):
                load_idx(b, b)
            sp.dma_start(wp[:, :], weights).then_inc(weights_in, 16)
            for b in range(2):
                load_pair(b, b)
                load_attr(b, b)
            sp.dma_start(dst_i[:, :, :], dst).then_inc(dst_in, 16)
            for c in range(CHUNKS):
                n = len(range(c, NB, CHUNKS))
                if c >= 2:
                    sp.wait_ge(bounds_step, 1 + 2 * (c - 1))
                sp.dma_start(rows_i[0:n, c % 2, :], dst_rows[c:NB:CHUNKS, :]
                             ).then_inc(rows_in[c % 2], 16)
            for b in range(2, IN_RING):
                load_pair(b, b)
                load_attr(b, b)
            sp.dma_start(x_late[:, :, :], x[N_EARLY:N, :].rearrange("(t p) d -> p t d", p=NP)
                         ).then_inc(x_late_in, 16)
            sp.wait_ge(bounds_step, 1 + 2 * CHUNKS)
            sp.dma_start(bounds_dram.rearrange("m (p c) -> p m c", p=P), bounds[:, :, :]
                         ).then_inc(bounds_out, 16)
            sp.wait_ge(bounds_out, 16)
            sp.dma_start(base_b[:, :], bounds_dram[0:1, 0:NB].broadcast_to([P, NB])
                         ).then_inc(base_in, 16)
            sp.dma_start(top[:, :], bounds_dram[1:2, 0:NB]).then_inc(base_in, 16)

            def ahead(b, s):
                sp.wait_ge(h0_done, b + 1)
                load_pair(b + IN_RING, s + IN_RING)
                sp.wait_ge(score_done, b + 1)
                load_attr(b + IN_RING, s + IN_RING)

            def ahead_all(b, s):
                ahead(b, s)
                sp.wait_ge(gathered[s % G_RING], uses(b, G_RING) * 16 * TILES)
                load_idx(b + G_RING, s + G_RING)

            blocks_loop(sp, 0, NB - G_RING, G_RING, ahead_all)
            for b in range(NB - G_RING, NB - IN_RING):
                ahead(b, b)

            for half in range(2):
                k0, k1 = half * len(groups) // 2, (half + 1) * len(groups) // 2
                c0, c1 = groups[k0][0], sum(groups[k1 - 1])
                sp.wait_ge(y_ready, k1)
                sp.dma_start(y_nodes[:, c0:c1, :], ln_y[:, c0:c1, :]).then_inc(y_out, 16)
            sp.wait_ge(y_ready, len(groups) + 1)
            sp.dma_start(out[N_EARLY:N, :].rearrange("(t p) d -> p t d", p=NP), y_late[:, :, :]
                         ).then_inc(y_out, 16)
            sp.wait_ge(y_out, 16 * 3)
            sp.wait_ge(h_out, 16 * LN_STEPS)

        @block.gpsimd
        def _(pool):
            pool.iota(iota_i[:, :], pattern=[[1, WIN]], base=0, channel_multiplier=0
                      ).then_inc(set_up, 1)

            def gather(b, s, table):
                slot = s % G_RING
                pool.wait_ge(idx_in[slot], uses(b, G_RING) * 16)
                pool.sem_inc(gathers_begun, 1)
                for t in range(tiles_of(b)):
                    pool.indirect_dma_start(
                        rows[:, slot, t, :], None, table,
                        bass.IndirectOffsetOnAxis(ap=idx[:, slot, t:t + 1], axis=0),
                    ).then_inc(gathered[slot], 16)

            for b in range(RAW):
                gather(b, b, x)
            pool.wait_ge(h_out, 16 * LN_STEPS)
            for b in range(RAW, G_RING):
                gather(b, b, h_dram)

            def gather_ahead(b, s):
                pool.wait_ge(msg_done, b + 1)
                gather(b + G_RING, s + G_RING, h_dram)

            blocks_loop(pool, 0, NB - G_RING, G_RING, gather_ahead)

        @block.scalar
        def _(act):
            def ln_act(k, n, parts):
                act.wait_ge(ln_centred, k + 1)
                if k >= 2:
                    act.wait_ge(ln_var_ready, k - 1)
                act.activation(ln_sq[0:parts, k % 2, 0:n, :], ln_d[0:parts, k % 4, 0:n, :],
                               ACT.Square).then_inc(ln_squared, 1)

            def ln_root(k, n, parts):
                act.wait_ge(ln_var_ready, k + 1)
                act.activation(ln_std[0:parts, k % 4, 0:n], ln_var[0:parts, k % 4, 0:n],
                               ACT.Sqrt).then_inc(ln_std_ready, 1)

            def store_h(k):
                act.wait_ge(h_ready, k + 1)
                cols = slice(k * LN_ROWS, (k + 1) * LN_ROWS)
                act.dma_start(h_nodes[:, cols, :], ln_d[0:NP, k % 4, :, :]).then_inc(h_out, 16)

            def gelus(b, s):
                act.wait_ge(h0_done, b + 1)
                act.activation(g1[:, s % 2, :], ps_h0[s % 2][:, :], ACT.Gelu, bias=b0
                               ).then_inc(g1_done, 1)
                act.wait_ge(h1_done, b + 1)
                for g in range(2):
                    act.activation(act_in[0:D, s % IN_RING, g, :],
                                   ps_h1[s % 2][g * D:(g + 1) * D, :], ACT.Gelu,
                                   bias=wp[g * D:(g + 1) * D, C_B1:C_B1 + 1]
                                   ).then_inc(g2_done, 1)

            act.wait_ge(fill_ready, 1)
            act.activation(act_in[D + DE:D + DE + 1, :, :, :].rearrange("p s g j -> p (s g j)"),
                           fill[D + DE:D + DE + 1, 1:2].to_broadcast([1, IN_RING * 2 * HALF]),
                           ACT.Copy).then_inc(ones_ready, 1)
            for k in range(LN_STEPS + 1):
                if k < LN_STEPS:
                    ln_act(k, *jobs[k])
                if k >= 1:
                    ln_root(k - 1, *jobs[k - 1])
                if k >= 2:
                    store_h(k - 2)
            store_h(LN_STEPS - 1)
            act.wait_ge(weights_in, 16)
            gelus(0, 0)
            act.activation(acc[:, :], fill[0:DC, 0:1].to_broadcast([DC, N + WIN]), ACT.Copy
                           ).then_inc(acc_zero, 1)
            for k in range(LN_STEPS, len(jobs) + 1):
                if k < len(jobs):
                    ln_act(k, *jobs[k])
                if k > LN_STEPS:
                    ln_root(k - 1, *jobs[k - 1])
            blocks_loop(act, 1, NB, IN_RING, gelus)

        @block.tensor
        def _(pe):
            pe.wait_ge(weights_in, 16)
            pe.matmul(ps_s[0][0:D + DE + 1, 0:D], wp[:, C_FOLD:C_FOLD + D + DE + 1],
                      wp[:, C_W3:C_W3 + D], start=True, stop=False)
            pe.matmul(ps_s[0][0:D + DE + 1, 0:D], wp[0:1, C_E:C_E + D + DE + 1],
                      wp[0:1, C_B3:C_B3 + D], start=False, stop=True).then_inc(fold_done, 1)

            def first(b, s):
                pe.wait_ge(pair_in[s % IN_RING], uses(b, IN_RING) * 16)
                pe.matmul(ps_h0[s % 2][:, :], w0, pair[:, s % IN_RING, :], start=True, stop=True
                          ).then_inc(h0_done, 1)

            def second(b, s):
                pe.wait_ge(g1_done, b + 1)
                pe.matmul(ps_h1[s % 2][:, :], w1, g1[:, s % 2, :], start=True, stop=True
                          ).then_inc(h1_done, 1)

            def last(b, s):
                pe.wait_ge(attr_in[s % IN_RING], uses(b, IN_RING) * 16)
                pe.wait_ge(g2_done, (b + 1) * 2)
                for t in range(TILES):
                    g, j = t % 2, t // 2
                    mm = pe.matmul(ps_s[s % 2][:, t * D:(t + 1) * D],
                                   act_in[:, s % IN_RING, g, j * P:(j + 1) * P],
                                   w_last[:, :], start=(t == 0), stop=(t == TILES - 1),
                                   skip_group_check=True)
                mm.then_inc(score_done, 1)

            def sums(b, s, window, onehot):
                n = tiles_of(b)
                for t in range(n):
                    last = pe.matmul(window, msg[:, s % 2, t, :], onehot[:, t, :],
                                     start=(t == 0), stop=(t == n - 1))
                return last

            def narrow(b, s):
                pe.wait_ge(msg_done, b + 1)
                if s == 0:
                    pe.wait_ge(first_hot, 1)
                sums(b, s, ps_w[s % 2][0:DC, 0:WIN], hot[:, s % 2, :, :]).then_inc(sums_done, 1)

            def wide(b, s):
                pe.wait_ge(msg_done, b + 1)
                spanned = pe.value_load(span[0:1, one(b)], min_val=0, max_val=N)
                with pe.Fori(0, (spanned >> WIN.bit_length() - 1) + 1) as w:
                    pe.wait_ge(win_hot, w + 1)
                    sums(b, s, ps_w[0][0:DC, 0:WIN], hot[:, 0, :, :]).then_inc(win_sums, 1)

            def project_early():
                pe.wait_ge(acc_done, 1)
                for k, (c, n) in enumerate(groups):
                    if k >= 2:
                        pe.wait_ge(y_mul, k - 1)
                    for j in range(n):
                        mm = pe.matmul(ps_h1[k % 2][0:EP, j * DC:(j + 1) * DC],
                                       acc[:, c + j:c + j + (EP - 1) * NC + 1:NC], wo,
                                       start=(j == 0), stop=(j == n - 1), skip_group_check=True)
                    mm.then_inc(proj_done, 1)
                pe.wait_ge(y_mul, len(groups))

            def project_late():
                pe.wait_ge(acc_done, 2)
                for t in range(LATE_TILES):
                    at = N_EARLY + t * NP
                    mm = pe.matmul(ps_h1[0][0:NP, t * DC:(t + 1) * DC], acc[:, at:at + NP], wo,
                                   start=(t == 0), stop=(t == LATE_TILES - 1), skip_group_check=True)
                mm.then_inc(proj_done, 1)

            def steps(first_block, end, summed):
                def step(b, s):
                    second(b, s)
                    first(b + 1, s + 1)
                    summed(b - 1, s - 1)
                    last(b, s)

                blocks_loop(pe, first_block, end, IN_RING, step)

            def finish(summed):
                second(NB - 1, NB - 1)
                summed(NB - 2, NB - 2)
                last(NB - 1, NB - 1)
                summed(NB - 1, NB - 1)

            first(0, 0)
            second(0, 0)
            first(1, 1)
            pe.wait_ge(w_last_ready, 1)
            pe.wait_ge(ones_ready, 1)
            last(0, 0)
            second(1, 1)
            first(2, 2)
            last(1, 1)
            pe.wait_ge(plan_ready, 1)
            flag = pe.value_load(widest[0:1, 0:1], min_val=0, max_val=N)
            with pe.If(flag < WIN):
                narrow(0, 0)
                steps(2, EARLY_BLOCKS + 1, narrow)
                project_early()
                steps(EARLY_BLOCKS + 1, NB - 1, narrow)
                finish(narrow)
            with pe.Else():
                wide(0, 0)
                steps(2, NB - 1, wide)
                finish(wide)
                project_early()
            project_late()

        @block.vector
        def _(dve):
            own = [0]

            def chained(ins):
                own[0] += 1
                ins.then_inc(ln_step, 1)
                dve.wait_ge(ln_step, own[0])

            dve.memset(fill[:, 0:1], 0.0)
            dve.memset(fill[:, 1:2], 1.0).then_inc(fill_ready, 1)
            dve.memset(msg[:, :, :, D:DC], 1.0)
            dve.memset(bounds[:, :, :], 0).then_inc(bounds_step, 1)
            dve.wait_ge(set_up, 1)
            dve.tensor_copy(iota[:, :], iota_i[:, :]).then_inc(set_up, 1)

            def source(k):
                if k < LN_STEPS:
                    return xs[:, k * LN_ROWS:(k + 1) * LN_ROWS, :]
                n = jobs[k][0]
                flat = rows[:, 0:RAW, :, :].rearrange("p b t d -> p (b t) d")
                return flat[:, (k - LN_STEPS) * n:(k - LN_STEPS + 1) * n, :]

            def centre(k):
                n, parts = jobs[k]
                d, s = ln_d[0:parts, k % 4, 0:n, :], ln_sum[0:parts, k % 4, 0:n]
                if k < LN_STEPS:
                    dve.wait_ge(x_in[k], 16)
                else:
                    per = RAW // (len(jobs) - LN_STEPS)
                    for b in range((k - LN_STEPS) * per, (k - LN_STEPS + 1) * per):
                        dve.wait_ge(gathered[b], 16 * TILES)
                    dve.wait_ge(h_out, 16 * LN_STEPS)
                chained(dve.tensor_reduce(s, source(k), AX_X, ALU.add))
                chained(dve.tensor_scalar(s, s, 1.0 / D, None, ALU.mult))
                dve.tensor_tensor(d, source(k), s.unsqueeze(2).to_broadcast([parts, n, D]),
                                  ALU.subtract).then_inc(ln_centred, 1)

            def variance(k):
                n, parts = jobs[k]
                v = ln_var[0:parts, k % 4, 0:n]
                dve.wait_ge(ln_squared, k + 1)
                chained(dve.tensor_reduce(v, ln_sq[0:parts, k % 2, 0:n, :], AX_X, ALU.add))
                dve.tensor_scalar(v, v, 1.0 / D, EPS, ALU.mult, ALU.add).then_inc(ln_var_ready, 1)

            def finish(k):
                n, parts = jobs[k]
                d, r = ln_d[0:parts, k % 4, 0:n, :], ln_std[0:parts, k % 4, 0:n]
                dve.wait_ge(ln_std_ready, k + 1)
                dve.wait_ge(ln_centred, k + 1)
                chained(dve.reciprocal(r, r))
                to = d if k < LN_STEPS else source(k)
                dve.scalar_tensor_tensor(out=to, in0=d, scalar=0.0,
                                         in1=r.unsqueeze(2).to_broadcast([parts, n, D]),
                                         op0=ALU.max, op1=ALU.mult
                                         ).then_inc(h_ready if k < LN_STEPS else raw_ready, 1)

            iota_tiles = iota[:, :].unsqueeze(1).to_broadcast([P, TILES, WIN])

            def one_hot(to, rel):
                return dve.tensor_tensor(to, rel.unsqueeze(2).to_broadcast([P, TILES, WIN]),
                                         iota_tiles, ALU.is_equal)

            def message(b, s):
                dve.wait_ge(score_done, b + 1)
                n = tiles_of(b)
                dve.wait_ge(gathered[s % G_RING], (uses(b, G_RING) - 1) * 16 * TILES + 16 * n)
                dve.tensor_tensor(msg[:, s % 2, 0:n, 0:D],
                                  ps_s[s % 2][:, 0:n * D].rearrange("p (t d) -> p t d", d=D),
                                  rows[:, s % G_RING, 0:n, :], ALU.mult).then_inc(msg_done, 1)

            def rel_of(b):
                return dst_rel[:, one(b), :].rearrange("p o t -> p (o t)")

            centre(0)
            for k in range(LN_STEPS):
                if k + 1 < LN_STEPS:
                    centre(k + 1)
                variance(k)
                finish(k)

            for c in range(CHUNKS):
                n = len(range(c, NB, CHUNKS))
                dve.wait_ge(rows_in[c % 2], 16 * (c // 2 + 1))
                if c == 0:
                    dve.wait_ge(bounds_step, 1)
                dve.tensor_reduce(bounds[0:n, 0, c:c + 1], rows_i[0:n, c % 2, :], AX_X, ALU.min
                                  ).then_inc(bounds_step, 1)
                dve.tensor_reduce(bounds[0:n, 1, c:c + 1], rows_i[0:n, c % 2, :], AX_X, ALU.max
                                  ).then_inc(bounds_step, 1)
            dve.wait_ge(fold_done, 1)
            dve.tensor_copy(w_last[:, :], ps_s[0][0:D + DE + 1, 0:D]).then_inc(w_last_ready, 1)

            centre(LN_STEPS)
            for k in range(LN_STEPS, len(jobs)):
                if k + 1 < len(jobs):
                    centre(k + 1)
                variance(k)
                finish(k)
                if k == LN_STEPS:
                    dve.wait_ge(raw_ready, 1)
                    message(0, 0)

            dve.wait_ge(base_in, 32)
            chained(dve.tensor_tensor(span[:, :], top[:, :], base_b[0:1, :], ALU.subtract))
            chained(dve.tensor_reduce(widest[:, :], span[:, :], AX_X, ALU.max))
            chained(dve.tensor_reduce(late[:, :], base_b[0:1, EARLY_BLOCKS:NB], AX_X, ALU.min))
            chained(dve.tensor_scalar(late[:, :], late[:, :], -1.0, float(N_EARLY + WIN - 1),
                                      ALU.mult, ALU.add))
            dve.tensor_tensor(widest[:, :], widest[:, :], late[:, :], ALU.max
                              ).then_inc(plan_ready, 1)
            dve.wait_ge(dst_in, 16)
            chained(dve.tensor_tensor(dst_rel, dst_i[:, :, :],
                                      base_b[:, :].unsqueeze(2).to_broadcast([P, NB, TILES]),
                                      ALU.subtract))
            dve.wait_ge(acc_zero, 1)
            dve.wait_ge(set_up, 2)
            dve.wait_ge(raw_ready, len(jobs) - LN_STEPS)
            dve.wait_ge(plan_ready, 1)

            def bias_residual():
                dve.tensor_tensor(xs[0:EP, :, :], xs[0:EP, :, :],
                                  bo[0:EP].unsqueeze(1).to_broadcast([EP, NC, D]), ALU.add
                                  ).then_inc(x_biased, 1)
                dve.wait_ge(x_late_in, 16)
                dve.tensor_tensor(x_late[:, :, :], x_late[:, :, :],
                                  bo.unsqueeze(1).to_broadcast([NP, LATE_TILES, D]), ALU.add
                                  ).then_inc(x_biased, 1)

            def output(k, got, n, parts, y, residual):
                dve.wait_ge(proj_done, k + 1)
                got = got[0:parts, 0:n * DC].rearrange("p (j d) -> p j d", d=DC)
                cnt = ln_sum[0:parts, k % 4, 0:n]
                dve.tensor_scalar(cnt.unsqueeze(2), got[:, :, D:DC], 1.0, None, ALU.max
                                  ).then_inc(cnt_ready, 1)
                dve.wait_ge(cnt_ready, 2 * k + 1)
                dve.reciprocal(cnt, cnt).then_inc(cnt_ready, 1)
                dve.wait_ge(cnt_ready, 2 * k + 2)
                dve.tensor_tensor(y, got[:, :, 0:D], cnt.unsqueeze(2).to_broadcast([parts, n, D]),
                                  ALU.mult).then_inc(y_mul, 1)
                dve.wait_ge(y_mul, k + 1)
                dve.tensor_tensor(y, y, residual, ALU.add).then_inc(y_ready, 1)

            def output_early():
                dve.sem_inc(acc_done, 1)
                dve.wait_ge(x_biased, 2)
                for k, (c, n) in enumerate(groups):
                    output(k, ps_h1[k % 2], n, EP, ln_y[:, c:c + n, :], xs[0:EP, c:c + n, :])

            def output_late():
                dve.sem_inc(acc_done, 1)
                output(len(groups), ps_h1[0], LATE_TILES, NP, y_late[:, :, :], x_late[:, :, :])

            def add_window(b, s):
                base = dve.value_load(base_b[0:1, one(b)], min_val=0, max_val=N - 1)
                dve.wait_ge(sums_done, b + 1)
                if s > 0:
                    dve.wait_ge(added, b)
                place = acc[:, bass.ds(base, WIN)]
                dve.tensor_tensor(place, place, ps_w[s % 2][0:DC, 0:WIN], ALU.add
                                  ).then_inc(added, 1)

            def narrow(b, s):
                one_hot(hot[:, s % 2, :, :], rel_of(b))
                message(b, s)

            def program_narrow():
                one_hot(hot[:, 0, :, :], rel_of(0)).then_inc(first_hot, 1)
                narrow(1, 1)
                add_window(0, 0)
                bias_residual()

                def step(b, s):
                    narrow(b, s)
                    add_window(b - 1, s - 1)

                blocks_loop(dve, 2, EARLY_BLOCKS + 1, G_RING, step)
                dve.wait_ge(added, EARLY_BLOCKS)
                output_early()
                blocks_loop(dve, EARLY_BLOCKS + 1, NB, G_RING, step)
                add_window(NB - 1, NB - 1)
                dve.wait_ge(added, NB)

            def wide(b, s):
                if s > 0:
                    message(b, s)
                base = dve.value_load(base_b[0:1, one(b)], min_val=0, max_val=N - 1)
                spanned = dve.value_load(span[0:1, one(b)], min_val=0, max_val=N)
                dve.tensor_copy(shifted[:, :], rel_of(b)).then_inc(win_shift, 1)
                with dve.Fori(0, (spanned >> WIN.bit_length() - 1) + 1) as w:
                    dve.wait_ge(win_shift, w * 2 + 1)
                    one_hot(hot[:, 0, :, :], shifted[:, :]).then_inc(win_hot, 1)
                    dve.wait_ge(win_hot, w + 1)
                    dve.tensor_scalar(shifted[:, :], shifted[:, :], float(-WIN), None, ALU.add
                                      ).then_inc(win_shift, 1)
                    dve.wait_ge(win_sums, w + 1)
                    at = nc.s_assert_within(
                        base + w * WIN, min_val=0, max_val=N,
                        skip_runtime_bounds_check_because="w * WIN is at most the block's span")
                    place = acc[:, bass.ds(at, WIN)]
                    dve.tensor_tensor(place, place, ps_w[0][0:DC, 0:WIN], ALU.add
                                      ).then_inc(win_shift, 1)
                dve.wait_ge(win_shift, ((spanned >> WIN.bit_length() - 1) + 1) * 2 + 1)
                dve.sem_inc(windows_ended, 1)
                dve.sem_clear(win_shift)
                dve.sem_clear(win_hot)
                dve.sem_clear(win_sums)

            flag = dve.value_load(widest[0:1, 0:1], min_val=0, max_val=N)
            with dve.If(flag < WIN):
                program_narrow()
            with dve.Else():
                bias_residual()
                wide(0, 0)
                blocks_loop(dve, 1, NB, G_RING, wide)
                output_early()

            output_late()


def one(b):
    return bass.ds(b, 1)


def kernel(x, src, dst, edge_attr_32, L0_gnn_W0, L0_gnn_b0, L0_gnn_W1, L0_gnn_b1, L0_gnn_W2,
           L0_gnn_b2, L0_gnn_W3, L0_gnn_b3, L0_gnn_Wo, L0_gnn_bo):
    import numpy as np
    import concourse.bacc as bacc
    from concourse.bass_utils import run_bass_kernel_spmd

    def padded(a, value):
        out = np.full((NB * BLOCK, *a.shape[1:]), value, a.dtype)
        out[:E] = a
        return out

    src, dst = np.asarray(src), np.asarray(dst)
    edges = padded(np.asarray(edge_attr_32), 0).reshape(NB, 2, HALF, DE).transpose(0, 1, 3, 2)
    tiled = lambda a: a.reshape(NB, 2, TILES // 2, P).transpose(0, 3, 2, 1).reshape(NB, P, TILES)
    dst_all = padded(dst, N)

    w = np.zeros((P, C_ALL), np.float32)
    for g in range(2):
        w[g * D:(g + 1) * D, C_W1 + g * D:C_W1 + (g + 1) * D] = L0_gnn_W1
        w[g * DE:(g + 1) * DE, C_W0 + g * D:C_W0 + (g + 1) * D] = L0_gnn_W0
        w[g * D:(g + 1) * D, C_W3:C_W3 + D] = L0_gnn_W3
        w[g * D:(g + 1) * D, C_B0] = L0_gnn_b0
        w[g * D:(g + 1) * D, C_B1] = L0_gnn_b1
    w[0:D, C_FOLD:C_FOLD + D] = np.asarray(L0_gnn_W2).T
    w[0:D, C_FOLD + D:C_FOLD + D + DE] = np.asarray(L0_gnn_W0).T
    w[0:D, C_FOLD + D + DE] = L0_gnn_b0
    w[D:2 * D, C_FOLD + D + DE] = L0_gnn_b2
    w[0:D, C_WO:C_WO + D] = L0_gnn_Wo
    w[D, C_WO + D] = 1.0
    w[0, C_E + D + DE] = 1.0
    w[0, C_B3:C_B3 + D] = L0_gnn_b3
    w[:, C_BO:C_BO + D] = L0_gnn_bo

    arrays = {
        "x": np.ascontiguousarray(x),
        "edges": np.ascontiguousarray(edges),
        "src": np.ascontiguousarray(tiled(padded(src, 0))),
        "dst": np.ascontiguousarray(tiled(dst_all).transpose(1, 0, 2)),
        "dst_rows": dst_all.reshape(NB, BLOCK),
        "weights": w,
    }
    nc = bacc.Bacc("TRN2", target_bir_lowering=False, num_devices=1)
    args = {n: nc.dram_tensor(f"in_{n}", a.shape, mybir.dt.from_np(a.dtype), kind="ExternalInput").ap()
            for n, a in arrays.items()}
    out = nc.dram_tensor("out", (N, D), F32, kind="ExternalOutput").ap()
    edge_gated_layer(nc, **args, out=out)
    got = run_bass_kernel_spmd(nc, [{f"in_{n}": a for n, a in arrays.items()}], core_ids=[0])
    return got.results[0]["out"]
```
